# Optimizing a Trainium2 kernel written in Bass

```python
import numpy as np
import jax
import jax.numpy as jnp

def _softmax(x, axis=-1):
    return jax.nn.softmax(x, axis=axis)

def _gelu(x):
    return jax.nn.gelu(x, approximate=True)

def _silu(x):
    return jax.nn.silu(x)

def _sigmoid(x):
    return jax.nn.sigmoid(x)

def _layernorm(x, axis=-1, eps=1e-05):
    m = jnp.mean(x, axis=axis, keepdims=True)
    v = jnp.var(x, axis=axis, keepdims=True)
    return (x - m) / jnp.sqrt(v + eps)

def _scatter_add(tgt, idx, src, axis=0):
    return tgt.at[idx].add(src)

def _segment_sum(src, seg, n):
    return jax.ops.segment_sum(src, seg, n)
kernel_name = 'mk_rec_standalone_d1_rec_r8_ae1365'

def setup_inputs(seed: int=0):
    np.random.seed(seed)
    _w = jnp.asarray

    def _rec_inputs():
        import jax
        import jax.numpy as jnp
        _rk = jax.random.key(seed)
        r_interactions = jnp.stack([jax.random.randint(jax.random.fold_in(jax.random.fold_in(_rk, 1), 0), (2048,), 1, 9997, jnp.int32), jax.random.randint(jax.random.fold_in(jax.random.fold_in(_rk, 1), 1), (2048,), 7, 1250, jnp.int32)], axis=1)
        return r_interactions
    r_interactions = _rec_inputs()

    def _L0_rec_setup():
        import jax, jax.numpy as jnp
        import numpy as np
        NUM_USERS = 12500
        NUM_ITEMS = 1250
        USER_DIM = 32
        ITEM_DIM = 32
        H1 = 128
        H2 = 128
        BATCH = 512
        key = jax.random.key(seed)
        ks = jax.random.split(key, 10)
        interactions = jax.random.randint(ks[0], (BATCH, 2), 0, NUM_ITEMS, dtype=jnp.int64)
        users_emb_w = jax.random.normal(ks[1], (NUM_USERS, USER_DIM), dtype=jnp.float32)
        items_emb_w = jax.random.normal(ks[2], (NUM_ITEMS, ITEM_DIM), dtype=jnp.float32)
        d_in = USER_DIM + ITEM_DIM
        w1 = jax.random.normal(ks[3], (H1, d_in), dtype=jnp.float32) / np.sqrt(d_in)
        b1 = jnp.zeros((H1,), dtype=jnp.float32)
        w2 = jax.random.normal(ks[4], (H2, H1), dtype=jnp.float32) / np.sqrt(H1)
        b2 = jnp.zeros((H2,), dtype=jnp.float32)
        head_in = NUM_ITEMS + H2
        w_head = jax.random.normal(ks[5], (NUM_ITEMS, head_in), dtype=jnp.float32) / np.sqrt(head_in)
        b_head = jnp.zeros((NUM_ITEMS,), dtype=jnp.float32)
        return {'interactions': interactions, 'users_emb_w': users_emb_w, 'items_emb_w': items_emb_w, 'w1': w1, 'b1': b1, 'w2': w2, 'b2': b2, 'w_head': w_head, 'b_head': b_head}
    _L0_rec_all = _L0_rec_setup()
    _L0_rec_in = {k: v for k, v in _L0_rec_all.items() if k in ('users_emb_w', 'items_emb_w', 'w1', 'b1', 'w2', 'b2', 'w_head', 'b_head')}
    del _L0_rec_all
    return {'r_interactions': r_interactions, 'L0_rec_users_emb_w': _L0_rec_in['users_emb_w'], 'L0_rec_items_emb_w': _L0_rec_in['items_emb_w'], 'L0_rec_w1': _L0_rec_in['w1'], 'L0_rec_b1': _L0_rec_in['b1'], 'L0_rec_w2': _L0_rec_in['w2'], 'L0_rec_b2': _L0_rec_in['b2'], 'L0_rec_w_head': _L0_rec_in['w_head'], 'L0_rec_b_head': _L0_rec_in['b_head']}

def reference(r_interactions, L0_rec_users_emb_w, L0_rec_items_emb_w, L0_rec_w1, L0_rec_b1, L0_rec_w2, L0_rec_b2, L0_rec_w_head, L0_rec_b_head):
    import jax
    import jax.numpy as jnp

    def _L0_rec_ref(interactions, users_emb_w, items_emb_w, w1, b1, w2, b2, w_head, b_head):
        import jax, jax.numpy as jnp
        import numpy as np
        NUM_USERS = 12500
        NUM_ITEMS = 1250
        USER_DIM = 32
        ITEM_DIM = 32
        H1 = 128
        H2 = 128
        BATCH = 512
        users = interactions[:, 0]
        items = interactions[:, 1]
        all_embed = jnp.concatenate([users_emb_w[users], items_emb_w[items]], axis=1)
        h = jax.nn.relu(all_embed @ w1.T + b1)
        h = jax.nn.relu(h @ w2.T + b2)
        cross = jax.nn.one_hot(items, NUM_ITEMS, dtype=h.dtype)
        head_in = jnp.concatenate([cross, h], axis=1)
        return jax.nn.sigmoid(head_in @ w_head.T + b_head)
    y = _L0_rec_ref(r_interactions, L0_rec_users_emb_w, L0_rec_items_emb_w, L0_rec_w1, L0_rec_b1, L0_rec_w2, L0_rec_b2, L0_rec_w_head, L0_rec_b_head)
    return y

_drawn_inputs = setup_inputs


def setup_inputs(seed=0):
    import zlib

    import numpy as np

    out = dict(_drawn_inputs(seed))
    spreads = {'L0_rec_b1': (0.0, 0.8), 'L0_rec_b2': (0.0, 0.762), 'L0_rec_b_head': (0.0, 0.1)}
    factors = {}
    for name, (base, spread) in spreads.items():
        noise = np.random.default_rng([zlib.crc32(name.encode()), seed]).standard_normal(out[name].shape)
        drawn = base * np.exp(spread * noise) if base else spread * noise
        out[name] = jnp.asarray(drawn.astype(out[name].dtype))
    for name, factor in factors.items():
        out[name] = (out[name] * factor).astype(out[name].dtype)
    return out
```

```python
from contextlib import ExitStack

import concourse.bass as bass
from concourse import mybir

P = 128
BANK = 512
TILES_PER_GROUP = 4
ACC_SLOTS = 2

ALU = mybir.AluOpType
ACT = mybir.ActivationFunctionType
F32 = mybir.dt.float32
BF16 = mybir.dt.bfloat16
I32 = mybir.dt.int32


def rec_head_kernel(nc, pairs, user_rows, item_rows, w1T, b1, w2T, b2, w_hiddenT, b_head, out):
    B = pairs.shape[0]
    UD = user_rows.shape[1]
    K1, H1 = w1T.shape
    H2, N = w_hiddenT.shape
    ID = K1 - UD
    ITEM_ROW = ID + N
    ROW = UD + ITEM_ROW
    TILES = B // P
    J = TILES_PER_GROUP
    GROUPS = TILES // J
    chunks = [(c, min(BANK, N - c)) for c in range(0, N, BANK)]
    BANKS = len(chunks)
    assert B % (P * J) == 0 and H1 == P and H2 == P and item_rows.shape[1] == ITEM_ROW

    pairs_v = pairs.rearrange("(p t) c -> p (t c)", p=P)
    out_v = out.rearrange("(p t) n -> p (t n)", p=P)

    with ExitStack() as ctx:
        def sb(name, shape, dt):
            return ctx.enter_context(nc.sbuf_tensor(name, shape, dt))

        def psum(name, shape, dt):
            return ctx.enter_context(nc.psum_tensor(name, shape, dt))

        def sem(name):
            return ctx.enter_context(nc.semaphore(name))

        rows = sb("rows", [P, TILES * ROW], F32)
        idx = sb("idx", [P, TILES * 2], I32)
        w1T_sb = sb("w1T_sb", [K1, H1], F32)
        w2T_sb = sb("w2T_sb", [H1, H2], F32)
        b1_sb = sb("b1_sb", [H1, 1], F32)
        b2_sb = sb("b2_sb", [H2, 1], F32)
        w_hidden_sb = sb("w_hidden_sb", [H2, N], F32)
        ident = sb("ident", [P, P], F32)
        emb = sb("emb", [P, J * P], F32)
        embT = sb("embT", [K1, J * P], F32)
        h1T = sb("h1T", [H1, J * P], F32)
        h2T = sb("h2T", [H2, J * P], F32)
        bias_f = sb("bias_f", [3, N], F32)
        bias_r = sb("bias_r", [3, N], F32)
        bias_p = sb("bias_p", [3, N], BF16)
        bias_q = sb("bias_q", [3, N], BF16)
        bias_parts = sb("bias_parts", [3, N], BF16)
        minus_after0 = sb("minus_after0", [3, 1], F32)
        minus_after1 = sb("minus_after1", [3, 1], F32)
        ones3 = sb("ones3", [3, P], BF16)

        acc = [psum(f"acc{s}", [P, BANKS * BANK], F32) for s in range(ACC_SLOTS)]
        psX = psum("psX", [P, BANK], F32)
        psY = psum("psY", [P, BANK], F32)

        s_idx = sem("s_idx")
        s_w1 = sem("s_w1")
        s_w2 = sem("s_w2")
        s_bias = sem("s_bias")
        s_hidden = sem("s_hidden")
        s_bhead = sem("s_bhead")
        s_rows = [sem(f"s_rows{j}") for j in range(J)]
        s_zero = sem("s_zero")
        s_ident = sem("s_ident")
        s_const = sem("s_const")
        s_split = sem("s_split")
        s_emb = sem("s_emb")
        s_xT = sem("s_xT")
        s_embT = sem("s_embT")
        s_l1 = sem("s_l1")
        s_h1 = sem("s_h1")
        s_l2 = sem("s_l2")
        s_h2 = sem("s_h2")
        s_acc_free = sem("s_acc_free")
        s_acc = sem("s_acc")
        s_sum = sem("s_sum")
        s_prob = sem("s_prob")
        s_out = sem("s_out")

        block = ctx.enter_context(nc.Block())

        @block.sync
        def _(sp):
            sp.dma_start(idx[:], pairs_v).then_inc(s_idx, 16)
            sp.dma_start(w1T_sb[:], w1T).then_inc(s_w1, 16)
            sp.dma_start(w2T_sb[:], w2T).then_inc(s_w2, 16)
            sp.dma_start(w_hidden_sb[:], w_hiddenT).then_inc(s_hidden, 16)

            def store(g, j):
                t = g * J + j
                sp.wait_ge(s_prob, t + 1)
                sp.dma_start(out_v[:, bass.ds(t * N, N)],
                             rows[:, bass.ds(t * ROW + K1, N)]).then_inc(s_out, 16)

            with sp.Fori(0, GROUPS) as g:
                for j in range(J):
                    store(g, j)
            sp.wait_ge(s_out, 16 * TILES)

        @block.gpsimd
        def _(pool):
            nc.gpsimd.memset(ident[:], 0.0).then_inc(s_zero, 1)
            pool.wait_ge(s_zero, 1)
            nc.gpsimd.affine_select(out=ident[:], in_=ident[:], compare_op=ALU.not_equal, fill=1.0, base=0,
                                    pattern=[[-1, P]], channel_multiplier=1).then_inc(s_ident, 1)
            pool.wait_ge(s_idx, 16)
            for g in range(GROUPS):
                for j in range(J):
                    t = g * J + j
                    if g > 0:
                        pool.wait_ge(s_rows[j], g * 32)
                    nc.gpsimd.indirect_dma_start(
                        out=rows[:, bass.ds(t * ROW, UD)], out_offset=None, in_=user_rows,
                        in_offset=bass.IndirectOffsetOnAxis(ap=idx[:, bass.ds(2 * t, 1)], axis=0),
                    ).then_inc(s_rows[j], 16)
                    nc.gpsimd.indirect_dma_start(
                        out=rows[:, bass.ds(t * ROW + UD, ITEM_ROW)], out_offset=None, in_=item_rows,
                        in_offset=bass.IndirectOffsetOnAxis(ap=idx[:, bass.ds(2 * t + 1, 1)], axis=0),
                    ).then_inc(s_rows[j], 16)

        @block.vector
        def _(dve):
            nc.vector.memset(emb[:], 0.0).then_inc(s_split, 1)
            nc.vector.memset(ones3[:], 1.0).then_inc(s_const, 1)
            nc.vector.memset(minus_after0[:], -1.0).then_inc(s_split, 1)
            nc.vector.memset(minus_after1[:], -1.0).then_inc(s_split, 1)
            dve.wait_ge(s_split, 3)
            nc.vector.memset(minus_after0[0:1, :], 0.0).then_inc(s_acc_free, 1)
            nc.vector.memset(minus_after1[0:2, :], 0.0).then_inc(s_acc_free, 1)
            dve.wait_ge(s_acc_free, 2)
            dve.wait_ge(s_bhead, 16)
            nc.vector.tensor_copy(bias_p[:], bias_f[:]).then_inc(s_split, 1)
            dve.wait_ge(s_split, 4)
            nc.vector.scalar_tensor_tensor(out=bias_r[:], in0=bias_p[:], scalar=minus_after0[:], in1=bias_f[:],
                                           op0=ALU.mult, op1=ALU.add).then_inc(s_split, 1)
            dve.wait_ge(s_split, 5)
            nc.vector.tensor_copy(bias_q[:], bias_r[:]).then_inc(s_split, 1)
            dve.wait_ge(s_split, 6)
            nc.vector.scalar_tensor_tensor(out=bias_parts[:], in0=bias_q[:], scalar=minus_after1[:], in1=bias_r[:],
                                           op0=ALU.mult, op1=ALU.add).then_inc(s_const, 1)

            def gather_embeddings(g):
                for j in range(J):
                    dve.wait_ge(s_rows[j], (g + 1) * 32)
                nc.vector.tensor_copy(
                    emb[:].rearrange("p (j k) -> p j k", j=J)[:, :, 0:K1],
                    rows[:, bass.ds(g * J * ROW, J * ROW)].rearrange("p (j r) -> p j r", j=J)[:, :, 0:K1],
                ).then_inc(s_emb, 1)

            def copy_embT(g):
                dve.wait_ge(s_xT, g + 1)
                nc.vector.tensor_copy(embT[:], psX[0:K1, 0:J * P]).then_inc(s_embT, 1)

            def add_rows(g, j):
                t = g * J + j
                dve.wait_ge(s_acc, t + 1)
                row = rows[:, bass.ds(t * ROW + K1, N)]
                nc.vector.tensor_tensor(row, acc[j % ACC_SLOTS][:, 0:N], row, ALU.add).then_inc(s_acc_free, 1)

            gather_embeddings(0)
            copy_embT(0)
            with dve.Fori(0, GROUPS - 1) as g:
                dve.wait_ge(s_l1, g + 1)
                gather_embeddings(g + 1)
                add_rows(g, 0)
                copy_embT(g + 1)
                for j in range(1, J):
                    add_rows(g, j)
            for j in range(J):
                add_rows(GROUPS - 1, j)

        @block.scalar
        def _(act):
            act.dma_start(b1_sb[:], b1.rearrange("(p a) -> p a", a=1)).then_inc(s_bias, 16)
            act.dma_start(b2_sb[:], b2.rearrange("(p a) -> p a", a=1)).then_inc(s_bias, 16)
            act.dma_start(bias_f[:], b_head.rearrange("(a n) -> a n", a=1).to_broadcast((3, N))).then_inc(s_bhead, 16)

            def relu_1(g):
                act.wait_ge(s_l1, g + 1)
                nc.scalar.activation(h1T[:], psY[:, 0:J * P], ACT.Relu, bias=b1_sb[:]).then_inc(s_h1, 1)

            def relu_2(j):
                nc.scalar.activation(h2T[:, j * P:(j + 1) * P], psX[:, j * P:(j + 1) * P], ACT.Relu,
                                     bias=b2_sb[:]).then_inc(s_h2, 1)

            def sigmoid(g, j):
                t = g * J + j
                act.wait_ge(s_acc_free, t + 1 + ACC_SLOTS)
                row = rows[:, bass.ds(t * ROW + K1, N)]
                nc.scalar.activation(row, row, ACT.Sigmoid).then_inc(s_prob, 1)

            act.wait_ge(s_bias, 32)
            relu_1(0)
            act.wait_ge(s_l2, 1)
            for j in range(J):
                relu_2(j)
            with act.Fori(0, GROUPS - 1) as g:
                sigmoid(g, 0)
                relu_1(g + 1)
                sigmoid(g, 1)
                act.wait_ge(s_l2, g + 2)
                act.wait_ge(s_acc, g * J + 3)
                for j in range(3):
                    relu_2(j)
                sigmoid(g, 2)
                act.wait_ge(s_acc, g * J + 4)
                relu_2(3)
                sigmoid(g, 3)
            for j in range(J):
                sigmoid(GROUPS - 1, j)

        @block.tensor
        def _(pe):
            def transpose(g):
                pe.wait_ge(s_emb, g + 1)
                for j in range(J):
                    last = nc.tensor.transpose(psX[:, j * P:(j + 1) * P], emb[:, j * P:(j + 1) * P], ident[:])
                last.then_inc(s_xT, 1)

            def layer_1(g):
                pe.wait_ge(s_embT, g + 1)
                nc.tensor.matmul(psY[:, 0:J * P], w1T_sb[:], embT[:], start=True, stop=True).then_inc(s_l1, 1)

            def layer_2(g):
                pe.wait_ge(s_h1, g + 1)
                nc.tensor.matmul(psX[:, 0:J * P], w2T_sb[:], h1T[:], start=True, stop=True).then_inc(s_l2, 1)

            def head(g, j):
                t = g * J + j
                pe.wait_ge(s_acc_free, t + 1)
                pe.wait_ge(s_h2, t + 1)
                a = acc[j % ACC_SLOTS]
                for c, n in chunks:
                    nc.tensor.matmul(a[:, c:c + n], h2T[:, j * P:(j + 1) * P], w_hidden_sb[:, c:c + n],
                                     start=True, stop=False)
                for c, n in chunks:
                    last = nc.tensor.matmul(a[:, c:c + n], ones3[:], bias_parts[:, c:c + n],
                                            start=False, stop=True)
                last.then_inc(s_acc, 1)

            pe.wait_ge(s_ident, 1)
            transpose(0)
            pe.wait_ge(s_w1, 16)
            layer_1(0)
            pe.wait_ge(s_w2, 16)
            layer_2(0)
            pe.wait_ge(s_hidden, 16)
            pe.wait_ge(s_const, 2)
            with pe.Fori(0, GROUPS - 1) as g:
                head(g, 0)
                pe.wait_ge(s_h2, (g + 1) * J)
                transpose(g + 1)
                head(g, 1)
                layer_1(g + 1)
                head(g, 2)
                layer_2(g + 1)
                head(g, 3)
            for j in range(J):
                head(GROUPS - 1, j)


def kernel(r_interactions, L0_rec_users_emb_w, L0_rec_items_emb_w, L0_rec_w1, L0_rec_b1, L0_rec_w2, L0_rec_b2,
           L0_rec_w_head, L0_rec_b_head):
    import numpy as np
    import concourse.bacc as bacc
    from concourse.bass_utils import run_bass_kernel_spmd

    n_items = L0_rec_w_head.shape[0]
    head = np.asarray(L0_rec_w_head)
    arrays = {
        "pairs": np.asarray(r_interactions),
        "user_rows": np.asarray(L0_rec_users_emb_w),
        "item_rows": np.concatenate([np.asarray(L0_rec_items_emb_w), head[:, :n_items].T], axis=1),
        "w1T": np.asarray(L0_rec_w1).T,
        "b1": np.asarray(L0_rec_b1),
        "w2T": np.asarray(L0_rec_w2).T,
        "b2": np.asarray(L0_rec_b2),
        "w_hiddenT": head[:, n_items:].T,
        "b_head": np.asarray(L0_rec_b_head),
    }
    arrays = {name: np.ascontiguousarray(a) for name, a in arrays.items()}

    nc = bacc.Bacc("TRN2", target_bir_lowering=False, num_devices=1)
    args = [nc.dram_tensor(name, a.shape, mybir.dt.from_np(a.dtype), kind="ExternalInput").ap()
            for name, a in arrays.items()]
    args.append(nc.dram_tensor("probs", (r_interactions.shape[0], n_items), F32, kind="ExternalOutput").ap())
    rec_head_kernel(nc, *args)
    r = run_bass_kernel_spmd(nc, [arrays], core_ids=[0])
    return r.results[0]["probs"]
```

```python
from contextlib import ExitStack

import concourse.bass as bass
from concourse import mybir

P = 128
BANK = 512
J = 2
IN_FLIGHT = 4

ALU = mybir.AluOpType
ACT = mybir.ActivationFunctionType
F32 = mybir.dt.float32
F32R = mybir.dt.float32r
I32 = mybir.dt.int32


def rec_head_kernel(nc, pairs, user_rows, item_rows, w1T, b1, w2T, b2, w_hiddenT, b_head, out):
    B = pairs.shape[0]
    UD = user_rows.shape[1]
    K1, H1 = w1T.shape
    H2, N = w_hiddenT.shape
    ID = K1 - UD
    ITEM_ROW = ID + N
    ROW = UD + ITEM_ROW
    TILES = B // P
    GROUPS = TILES // J
    GP = J * P
    chunks = [(c, min(BANK, N - c)) for c in range(0, N, BANK)]
    BANKS = len(chunks)
    assert B % (P * J) == 0 and H1 == P and H2 == P and 2 * K1 == P and item_rows.shape[1] == ITEM_ROW
    assert GROUPS % 2 == 0 and GROUPS >= 6 and IN_FLIGHT == 2 * J

    pairs_v = pairs.rearrange("(p t) c -> p (t c)", p=P)
    out_v = out.rearrange("(p t) n -> p (t n)", p=P)

    with ExitStack() as ctx:
        def sb(name, shape, dt):
            return ctx.enter_context(nc.sbuf_tensor(name, shape, dt))

        def psum(name, shape, dt):
            return ctx.enter_context(nc.psum_tensor(name, shape, dt))

        def sem(name):
            return ctx.enter_context(nc.semaphore(name))

        rows = sb("rows", [P, TILES * ROW], F32)
        idx = sb("idx", [P, TILES * 2], I32)
        ident = sb("ident", [P, P], F32)
        w1T_f = sb("w1T_f", [2 * K1, H1], F32)
        w1T_hi = sb("w1T_hi", [2 * K1, H1], F32R)
        w1T_lo = sb("w1T_lo", [2 * K1, H1], F32R)
        w2T_sb = sb("w2T_sb", [H1, H2], F32)
        b1_sb = sb("b1_sb", [H1, 1], F32)
        b2_sb = sb("b2_sb", [H2, 1], F32)
        w_hid_f = sb("w_hid_f", [H2, N], F32)
        w_hid_hi = sb("w_hid_hi", [H2, N], F32R)
        w_hid_lo = sb("w_hid_lo", [H2, N], F32R)
        bias_f = sb("bias_f", [2, N], F32)
        bias_hi = sb("bias_hi", [2, N], F32R)
        bias_parts = sb("bias_parts", [P, N], F32R)
        bias_sel = sb("bias_sel", [P, P], F32R)
        minus_on_lo = sb("minus_on_lo", [2, 1], F32)
        warm = sb("warm", [P, 1], F32)
        emb = sb("emb", [P, J * 2 * K1], F32)
        embT = sb("embT", [2 * K1, GP], F32R)
        h1T = sb("h1T", [H1, GP], F32)
        h2T_f = sb("h2T_f", [H2, GP], F32)
        h2T_hi = sb("h2T_hi", [H2, GP], F32R)
        h2T_lo = sb("h2T_lo", [H2, GP], F32R)

        acc = [psum(f"acc{s}", [P, BANKS * BANK], F32) for s in range(J)]
        ps_in = psum("ps_in", [P, BANK], F32)
        ps_l2 = psum("ps_l2", [P, BANK], F32)

        s_idx = sem("s_idx")
        s_w1 = sem("s_w1")
        s_w2 = sem("s_w2")
        s_b12 = sem("s_b12")
        s_hidden = sem("s_hidden")
        s_bhead = sem("s_bhead")
        s_rows = [sem(f"s_rows{i}") for i in range(IN_FLIGHT)]
        s_zero = sem("s_zero")
        s_ident = sem("s_ident")
        s_const = sem("s_const")
        s_w1_parts = sem("s_w1_parts")
        s_hid_hi = sem("s_hid_hi")
        s_hid_lo = sem("s_hid_lo")
        s_bias_parts = sem("s_bias_parts")
        s_emb_hi = sem("s_emb_hi")
        s_emb = sem("s_emb")
        s_xT = sem("s_xT")
        s_embT = sem("s_embT")
        s_l1 = sem("s_l1")
        s_h1 = sem("s_h1")
        s_l2 = sem("s_l2")
        s_h2 = sem("s_h2")
        s_h2_lo = sem("s_h2_lo")
        s_acc_free = sem("s_acc_free")
        s_acc = sem("s_acc")
        s_prob = sem("s_prob")
        s_out = sem("s_out")
        s_last_acc = sem("s_last_acc")
        s_last_sum = sem("s_last_sum")
        s_last_prob = sem("s_last_prob")

        def logits(t):
            return rows[:, bass.ds(t * ROW + K1, N)]

        def last_logits(c, n):
            at = (TILES - 1) * ROW + K1 + c
            return rows[:, at:at + n]

        block = ctx.enter_context(nc.Block())

        @block.sync
        def _(sp):
            sp.dma_start(idx[:], pairs_v).then_inc(s_idx, 16)
            sp.dma_start(w_hid_f[:], w_hiddenT).then_inc(s_hidden, 16)
            sp.dma_start(w2T_sb[:], w2T).then_inc(s_w2, 16)
            with sp.Fori(0, TILES - 1) as t:
                sp.wait_ge(s_prob, t + 1)
                sp.dma_start(out_v[:, bass.ds(t * N, N)], logits(t)).then_inc(s_out, 16)
            for i, (c, n) in enumerate(chunks):
                sp.wait_ge(s_last_prob, i + 1)
                at = (TILES - 1) * N + c
                sp.dma_start(out_v[:, at:at + n], last_logits(c, n)).then_inc(s_out, 16)
            sp.wait_ge(s_out, 16 * (TILES - 1 + BANKS))

        @block.gpsimd
        def _(pool):
            nc.gpsimd.memset(ident[:], 0.0).then_inc(s_zero, 1)
            pool.wait_ge(s_zero, 1)
            nc.gpsimd.affine_select(out=ident[:], in_=ident[:], compare_op=ALU.not_equal, fill=1.0, base=0,
                                    pattern=[[-1, P]], channel_multiplier=1).then_inc(s_ident, 1)
            pool.wait_ge(s_idx, 16)
            for t in range(TILES):
                landed = s_rows[t % IN_FLIGHT]
                if t >= IN_FLIGHT:
                    pool.wait_ge(landed, 32 * (t // IN_FLIGHT))
                at = t * ROW
                nc.gpsimd.indirect_dma_start(
                    out=rows[:, at:at + UD], out_offset=None, in_=user_rows,
                    in_offset=bass.IndirectOffsetOnAxis(ap=idx[:, 2 * t:2 * t + 1], axis=0),
                ).then_inc(landed, 16)
                nc.gpsimd.indirect_dma_start(
                    out=rows[:, at + UD:at + ROW], out_offset=None, in_=item_rows,
                    in_offset=bass.IndirectOffsetOnAxis(ap=idx[:, 2 * t + 1:2 * t + 2], axis=0),
                ).then_inc(landed, 16)

        @block.vector
        def _(dve):
            nc.vector.memset(warm[:], 0.0).then_inc(s_const, 1)
            nc.vector.memset(minus_on_lo[:], -1.0).then_inc(s_const, 1)
            nc.vector.memset(bias_sel[:].bitcast(F32), 0.0).then_inc(s_acc_free, 1)
            nc.vector.memset(bias_parts[:].bitcast(F32), 0.0).then_inc(s_acc_free, 1)
            dve.wait_ge(s_const, 2)
            nc.vector.memset(minus_on_lo[0:1, :], 0.0).then_inc(s_const, 1)
            dve.wait_ge(s_acc_free, 2)
            nc.vector.memset(bias_sel[0:2, :].bitcast(F32), 1.0).then_inc(s_const, 1)
            dve.wait_ge(s_w1, 32)
            nc.vector.tensor_copy(w1T_hi[:], w1T_f[:]).then_inc(s_w1_parts, 1)
            dve.wait_ge(s_w1_parts, 1)
            nc.vector.tensor_tensor(w1T_lo[:], w1T_f[:], w1T_hi[:].bitcast(F32), ALU.subtract).then_inc(s_w1_parts, 1)
            dve.wait_ge(s_bhead, 16)
            dve.wait_ge(s_const, 4)
            nc.vector.tensor_copy(bias_hi[:], bias_f[:]).then_inc(s_bias_parts, 1)
            dve.wait_ge(s_bias_parts, 1)
            nc.vector.scalar_tensor_tensor(
                out=bias_parts[0:2, :], in0=bias_hi[:].bitcast(F32), scalar=minus_on_lo[:], in1=bias_f[:],
                op0=ALU.mult, op1=ALU.add).then_inc(s_bias_parts, 1)
            dve.wait_ge(s_hid_hi, 1)
            nc.vector.tensor_tensor(w_hid_lo[:], w_hid_f[:], w_hid_hi[:].bitcast(F32),
                                    ALU.subtract).then_inc(s_hid_lo, 1)

            def split_embeddings(g, first, nth):
                for j in range(J):
                    dve.wait_ge(s_rows[first + j], nth * 32)
                tiles = rows[:, bass.ds(g * J * ROW, J * ROW)].rearrange("p (j r) -> p j r", j=J)[:, :, 0:K1]
                parts = emb[:].rearrange("p (j s k) -> p j s k", j=J, s=2)
                nc.vector.tensor_copy(parts[:, :, 0, :].bitcast(F32R), tiles).then_inc(s_emb_hi, 1)
                dve.wait_ge(s_emb_hi, g + 1)
                nc.vector.tensor_tensor(parts[:, :, 1, :], tiles, parts[:, :, 0, :], ALU.subtract).then_inc(s_emb, 1)

            def copy_embT(g):
                dve.wait_ge(s_xT, g + 1)
                nc.vector.tensor_copy(embT[:], ps_in[:, 0:GP]).then_inc(s_embT, 1)

            def split_h2(g, j):
                dve.wait_ge(s_h2, g * J + j + 1)
                at = slice(j * P, (j + 1) * P)
                nc.vector.tensor_tensor(h2T_lo[:, at], h2T_f[:, at], h2T_hi[:, at].bitcast(F32),
                                        ALU.subtract).then_inc(s_h2_lo, 1)

            def add_rows(g, j):
                t = g * J + j
                dve.wait_ge(s_acc, t + 1)
                nc.vector.tensor_tensor(logits(t), acc[j][:, 0:N], logits(t), ALU.add).then_inc(s_acc_free, 1)

            def step(g, first, nth):
                split_embeddings(g + 2, first, nth)
                add_rows(g, 0)
                split_h2(g + 1, 0)
                copy_embT(g + 2)
                add_rows(g, 1)
                split_h2(g + 1, 1)

            split_embeddings(0, 0, 1)
            copy_embT(0)
            split_h2(0, 0)
            split_h2(0, 1)
            split_embeddings(1, J, 1)
            copy_embT(1)
            step(0, 0, 2)
            with dve.Fori(0, (GROUPS - 4) // 2) as i:
                step(2 * i + 1, J, i + 2)
                step(2 * i + 2, 0, i + 3)
            step(GROUPS - 3, J, TILES // IN_FLIGHT)
            for j in range(J):
                add_rows(GROUPS - 2, j)
                split_h2(GROUPS - 1, j)
            add_rows(GROUPS - 1, 0)
            for i, (c, n) in enumerate(chunks):
                dve.wait_ge(s_last_acc, i + 1)
                nc.vector.tensor_tensor(last_logits(c, n), acc[J - 1][:, c:c + n], last_logits(c, n),
                                        ALU.add).then_inc(s_last_sum, 1)

        @block.scalar
        def _(act):
            for half in range(2):
                act.dma_start(w1T_f[half * K1:(half + 1) * K1, :], w1T).then_inc(s_w1, 16)
            act.dma_start(b1_sb[:], b1.rearrange("(p a) -> p a", a=1)).then_inc(s_b12, 16)
            act.dma_start(bias_f[:], b_head.rearrange("(a n) -> a n", a=1).to_broadcast((2, N))).then_inc(s_bhead, 16)
            act.dma_start(b2_sb[:], b2.rearrange("(p a) -> p a", a=1)).then_inc(s_b12, 16)
            act.wait_ge(s_const, 1)
            nc.scalar.activation(warm[:], warm[:], ACT.Sigmoid)
            act.wait_ge(s_hidden, 16)
            nc.scalar.activation(w_hid_hi[:], w_hid_f[:], ACT.Copy).then_inc(s_hid_hi, 1)

            def relu_1(g):
                act.wait_ge(s_l1, g + 1)
                nc.scalar.activation(h1T[:], ps_in[:, 0:GP], ACT.Relu, bias=b1_sb[:]).then_inc(s_h1, 1)

            def relu_2(j):
                at = slice(j * P, (j + 1) * P)
                nc.scalar.activation(h2T_hi[:, at], ps_l2[:, at], ACT.Relu, bias=b2_sb[:])
                nc.scalar.activation(h2T_f[:, at], ps_l2[:, at], ACT.Relu, bias=b2_sb[:]).then_inc(s_h2, 1)

            def sigmoid(g, j):
                t = g * J + j
                act.wait_ge(s_acc_free, t + 1 + J)
                nc.scalar.activation(logits(t), logits(t), ACT.Sigmoid).then_inc(s_prob, 1)

            def step(g, with_l1):
                act.wait_ge(s_l2, g + 2)
                act.wait_ge(s_acc, g * J + 1)
                relu_2(0)
                sigmoid(g, 0)
                act.wait_ge(s_acc, g * J + 2)
                relu_2(1)
                if with_l1:
                    relu_1(g + 2)
                sigmoid(g, 1)

            act.wait_ge(s_b12, 32)
            relu_1(0)
            act.wait_ge(s_l2, 1)
            relu_2(0)
            relu_2(1)
            relu_1(1)
            with act.Fori(0, GROUPS - 2) as g:
                step(g, True)
            step(GROUPS - 2, False)
            sigmoid(GROUPS - 1, 0)
            for i, (c, n) in enumerate(chunks):
                act.wait_ge(s_last_sum, i + 1)
                nc.scalar.activation(last_logits(c, n), last_logits(c, n), ACT.Sigmoid).then_inc(s_last_prob, 1)

        @block.tensor
        def _(pe):
            def transpose(g):
                pe.wait_ge(s_emb, g + 1)
                for j in range(J):
                    last = nc.tensor.transpose(ps_in[:, j * P:(j + 1) * P], emb[:, j * P:(j + 1) * P], ident[:])
                last.then_inc(s_xT, 1)

            def layer_1(g):
                pe.wait_ge(s_embT, g + 1)
                nc.tensor.matmul(ps_in[:, 0:GP], w1T_hi[:], embT[:], start=True, stop=False)
                nc.tensor.matmul(ps_in[:, 0:GP], w1T_lo[:], embT[:], start=False, stop=True).then_inc(s_l1, 1)

            def layer_2(g):
                pe.wait_ge(s_h1, g + 1)
                nc.tensor.matmul(ps_l2[:, 0:GP], w2T_sb[:], h1T[:], start=True, stop=True).then_inc(s_l2, 1)

            def products(j):
                at = slice(j * P, (j + 1) * P)
                return [(h2T_hi[:, at], w_hid_hi), (h2T_hi[:, at], w_hid_lo), (h2T_lo[:, at], w_hid_hi),
                        (bias_sel[:], bias_parts)]

            def head(g, j):
                t = g * J + j
                pe.wait_ge(s_acc_free, t + 1)
                pe.wait_ge(s_h2_lo, t + 1)
                terms = products(j)
                for k, (h, w) in enumerate(terms):
                    for c, n in chunks:
                        last = nc.tensor.matmul(acc[j][:, c:c + n], h, w[:, c:c + n],
                                                start=(k == 0), stop=(k == len(terms) - 1))
                last.then_inc(s_acc, 1)

            def last_head():
                pe.wait_ge(s_acc_free, TILES)
                pe.wait_ge(s_h2_lo, TILES)
                terms = products(J - 1)
                for c, n in chunks:
                    for k, (h, w) in enumerate(terms):
                        last = nc.tensor.matmul(acc[J - 1][:, c:c + n], h, w[:, c:c + n],
                                                start=(k == 0), stop=(k == len(terms) - 1))
                    last.then_inc(s_last_acc, 1)

            def step(g, with_l1):
                head(g, 0)
                layer_2(g + 1)
                if with_l1:
                    transpose(g + 2)
                head(g, 1)
                if with_l1:
                    layer_1(g + 2)

            pe.wait_ge(s_ident, 1)
            transpose(0)
            pe.wait_ge(s_w1_parts, 2)
            layer_1(0)
            pe.wait_ge(s_w2, 16)
            layer_2(0)
            transpose(1)
            layer_1(1)
            pe.wait_ge(s_hid_lo, 1)
            pe.wait_ge(s_bias_parts, 2)
            with pe.Fori(0, GROUPS - 2) as g:
                step(g, True)
            step(GROUPS - 2, False)
            head(GROUPS - 1, 0)
            last_head()


def kernel(r_interactions, L0_rec_users_emb_w, L0_rec_items_emb_w, L0_rec_w1, L0_rec_b1, L0_rec_w2, L0_rec_b2,
           L0_rec_w_head, L0_rec_b_head):
    import numpy as np
    import concourse.bacc as bacc
    from concourse.bass_utils import run_bass_kernel_spmd

    n_items = L0_rec_w_head.shape[0]
    head = np.asarray(L0_rec_w_head)
    arrays = {
        "pairs": np.asarray(r_interactions),
        "user_rows": np.asarray(L0_rec_users_emb_w),
        "item_rows": np.concatenate([np.asarray(L0_rec_items_emb_w), head[:, :n_items].T], axis=1),
        "w1T": np.asarray(L0_rec_w1).T,
        "b1": np.asarray(L0_rec_b1),
        "w2T": np.asarray(L0_rec_w2).T,
        "b2": np.asarray(L0_rec_b2),
        "w_hiddenT": head[:, n_items:].T,
        "b_head": np.asarray(L0_rec_b_head),
    }
    arrays = {name: np.ascontiguousarray(a) for name, a in arrays.items()}

    nc = bacc.Bacc("TRN2", target_bir_lowering=False, num_devices=1)
    args = [nc.dram_tensor(name, a.shape, mybir.dt.from_np(a.dtype), kind="ExternalInput").ap()
            for name, a in arrays.items()]
    args.append(nc.dram_tensor("probs", (r_interactions.shape[0], n_items), F32, kind="ExternalOutput").ap())
    rec_head_kernel(nc, *args)
    r = run_bass_kernel_spmd(nc, [arrays], core_ids=[0])
    return r.results[0]["probs"]
```

```python
from contextlib import ExitStack

import concourse.bass as bass
from concourse import mybir

P = 128
BANK = 512
J = 2
IN_FLIGHT = 4

ALU = mybir.AluOpType
ACT = mybir.ActivationFunctionType
F32 = mybir.dt.float32
F32R = mybir.dt.float32r
I32 = mybir.dt.int32


def rec_head_kernel(nc, pairs, user_rows, item_rows, w1T, b1, w2T, b2, w_hiddenT, b_head, out):
    B = pairs.shape[0]
    UD = user_rows.shape[1]
    K1, H1 = w1T.shape
    H2, N = w_hiddenT.shape
    ID = K1 - UD
    ITEM_ROW = ID + N
    ROW = UD + ITEM_ROW
    TILES = B // P
    GROUPS = TILES // J
    GP = J * P
    chunks = [(c, min(BANK, N - c)) for c in range(0, N, BANK)]
    BANKS = len(chunks)
    assert B % (P * J) == 0 and H1 == P and H2 == P and 2 * K1 == P and item_rows.shape[1] == ITEM_ROW
    assert GROUPS % 2 == 0 and GROUPS >= 6 and IN_FLIGHT == 2 * J

    pairs_v = pairs.rearrange("(p t) c -> p (t c)", p=P)
    out_v = out.rearrange("(p t) n -> p (t n)", p=P)

    with ExitStack() as ctx:
        def sb(name, shape, dt):
            return ctx.enter_context(nc.sbuf_tensor(name, shape, dt))

        def psum(name, shape, dt):
            return ctx.enter_context(nc.psum_tensor(name, shape, dt))

        def sem(name):
            return ctx.enter_context(nc.semaphore(name))

        rows = sb("rows", [P, TILES * ROW], F32)
        idx = sb("idx", [P, TILES * 2], I32)
        ident = sb("ident", [P, P], F32)
        w1T_f = sb("w1T_f", [2 * K1, H1], F32)
        w1T_hi = sb("w1T_hi", [2 * K1, H1], F32R)
        w1T_lo = sb("w1T_lo", [2 * K1, H1], F32R)
        w2T_sb = sb("w2T_sb", [H1, H2], F32)
        b1_sb = sb("b1_sb", [H1, 1], F32)
        b2_sb = sb("b2_sb", [H2, 1], F32)
        w_hid_f = sb("w_hid_f", [H2, N], F32)
        w_hid_hi = sb("w_hid_hi", [H2, N], F32R)
        w_hid_lo = sb("w_hid_lo", [H2, N], F32R)
        bias_f = sb("bias_f", [2, N], F32)
        bias_hi = sb("bias_hi", [2, N], F32R)
        bias_parts = sb("bias_parts", [P, N], F32R)
        bias_sel = sb("bias_sel", [P, P], F32R)
        bias_all = sb("bias_all", [P, N], F32)
        ones = sb("ones", [1, P], F32)
        minus_on_lo = sb("minus_on_lo", [2, 1], F32)
        warm = sb("warm", [P, 1], F32)
        emb = sb("emb", [P, J * 2 * K1], F32)
        embT = sb("embT", [2 * K1, GP], F32R)
        h1T = sb("h1T", [H1, GP], F32)
        h2T_f = sb("h2T_f", [H2, GP], F32)
        h2T_hi = sb("h2T_hi", [H2, GP], F32R)
        h2T_lo = sb("h2T_lo", [H2, GP], F32R)

        acc = [psum(f"acc{s}", [P, BANKS * BANK], F32) for s in range(J)]
        ps_in = psum("ps_in", [P, BANK], F32)
        ps_l2 = psum("ps_l2", [P, BANK], F32)

        s_idx = sem("s_idx")
        s_w1 = sem("s_w1")
        s_w2 = sem("s_w2")
        s_b1_b2 = sem("s_b1_b2")
        s_w_hid = sem("s_w_hid")
        s_bhead = sem("s_bhead")
        s_rows = [sem(f"s_rows{i}") for i in range(IN_FLIGHT)]
        s_zero = sem("s_zero")
        s_ident = sem("s_ident")
        s_const = sem("s_const")
        s_w1_parts = sem("s_w1_parts")
        s_w_hid_hi = sem("s_w_hid_hi")
        s_w_hid_lo = sem("s_w_hid_lo")
        s_bias_parts = sem("s_bias_parts")
        s_bias_spread = sem("s_bias_spread")
        s_bias_all = sem("s_bias_all")
        s_biased = sem("s_biased")
        s_emb_hi = sem("s_emb_hi")
        s_emb = sem("s_emb")
        s_transposed = sem("s_transposed")
        s_embT = sem("s_embT")
        s_l1 = sem("s_l1")
        s_h1 = sem("s_h1")
        s_l2 = sem("s_l2")
        s_h2 = sem("s_h2")
        s_h2_lo = sem("s_h2_lo")
        s_acc_free = sem("s_acc_free")
        s_acc = sem("s_acc")
        s_probs = sem("s_probs")
        s_out = sem("s_out")
        s_last_acc = sem("s_last_acc")
        s_last_sum = sem("s_last_sum")
        s_last_probs = sem("s_last_probs")

        def logits(t):
            return rows[:, bass.ds(t * ROW + K1, N)]

        def last_logits(c, n):
            at = (TILES - 1) * ROW + K1 + c
            return rows[:, at:at + n]

        block = ctx.enter_context(nc.Block())

        @block.sync
        def _(sp):
            sp.dma_start(idx[:], pairs_v).then_inc(s_idx, 16)
            sp.dma_start(bias_f[:], b_head.rearrange("(a n) -> a n", a=1).to_broadcast((2, N))).then_inc(s_bhead, 16)
            sp.dma_start(w1T_f[0:K1, :], w1T).then_inc(s_w1, 16)
            sp.dma_start(w2T_sb[:], w2T).then_inc(s_w2, 16)
            with sp.Fori(0, TILES - 1) as t:
                sp.wait_ge(s_probs, t + 1)
                sp.dma_start(out_v[:, bass.ds(t * N, N)], logits(t)).then_inc(s_out, 16)
            for i, (c, n) in enumerate(chunks):
                sp.wait_ge(s_last_probs, i + 1)
                at = (TILES - 1) * N + c
                sp.dma_start(out_v[:, at:at + n], last_logits(c, n)).then_inc(s_out, 16)
            sp.wait_ge(s_out, 16 * (TILES - 1 + BANKS))

        @block.gpsimd
        def _(pool):
            nc.gpsimd.memset(ident[:], 0.0).then_inc(s_zero, 1)
            pool.wait_ge(s_zero, 1)
            nc.gpsimd.affine_select(out=ident[:], in_=ident[:], compare_op=ALU.not_equal, fill=1.0, base=0,
                                    pattern=[[-1, P]], channel_multiplier=1).then_inc(s_ident, 1)
            pool.wait_ge(s_idx, 16)
            for t in range(TILES):
                landed = s_rows[t % IN_FLIGHT]
                if t >= IN_FLIGHT:
                    pool.wait_ge(landed, 32 * (t // IN_FLIGHT))
                at = t * ROW
                nc.gpsimd.indirect_dma_start(
                    out=rows[:, at + UD:at + ROW], out_offset=None, in_=item_rows,
                    in_offset=bass.IndirectOffsetOnAxis(ap=idx[:, 2 * t + 1:2 * t + 2], axis=0),
                ).then_inc(landed, 16)
                nc.gpsimd.indirect_dma_start(
                    out=rows[:, at:at + UD], out_offset=None, in_=user_rows,
                    in_offset=bass.IndirectOffsetOnAxis(ap=idx[:, 2 * t:2 * t + 1], axis=0),
                ).then_inc(landed, 16)

        @block.vector
        def _(dve):
            nc.vector.memset(ones[:], 1.0).then_inc(s_const, 1)
            nc.vector.memset(warm[:], 0.0).then_inc(s_const, 1)
            nc.vector.memset(minus_on_lo[:], -1.0).then_inc(s_const, 1)
            nc.vector.memset(bias_sel[:].bitcast(F32), 0.0).then_inc(s_const, 1)
            nc.vector.memset(bias_parts[:].bitcast(F32), 0.0).then_inc(s_acc_free, 1)
            dve.wait_ge(s_const, 4)
            nc.vector.memset(minus_on_lo[0:1, :], 0.0).then_inc(s_const, 1)
            nc.vector.memset(bias_sel[0:2, :].bitcast(F32), 1.0).then_inc(s_const, 1)
            dve.wait_ge(s_w1, 32)
            nc.vector.tensor_copy(w1T_hi[:], w1T_f[:]).then_inc(s_w1_parts, 1)
            dve.wait_ge(s_w1_parts, 1)
            nc.vector.tensor_tensor(w1T_lo[:], w1T_f[:], w1T_hi[:].bitcast(F32), ALU.subtract).then_inc(s_w1_parts, 1)
            dve.wait_ge(s_bhead, 16)
            dve.wait_ge(s_const, 6)
            dve.wait_ge(s_acc_free, 1)
            nc.vector.tensor_copy(bias_hi[:], bias_f[:]).then_inc(s_bias_parts, 1)
            dve.wait_ge(s_bias_parts, 1)
            nc.vector.scalar_tensor_tensor(
                out=bias_parts[0:2, :], in0=bias_hi[:].bitcast(F32), scalar=minus_on_lo[:], in1=bias_f[:],
                op0=ALU.mult, op1=ALU.add).then_inc(s_bias_parts, 1)
            dve.wait_ge(s_w_hid_hi, 1)
            nc.vector.tensor_tensor(w_hid_lo[:], w_hid_f[:], w_hid_hi[:].bitcast(F32),
                                    ALU.subtract).then_inc(s_w_hid_lo, 1)

            def split_embeddings(g, first, nth):
                for j in range(J):
                    dve.wait_ge(s_rows[first + j], nth * 32)
                tiles = rows[:, bass.ds(g * J * ROW, J * ROW)].rearrange("p (j r) -> p j r", j=J)[:, :, 0:K1]
                parts = emb[:].rearrange("p (j s k) -> p j s k", j=J, s=2)
                nc.vector.tensor_copy(parts[:, :, 0, :].bitcast(F32R), tiles).then_inc(s_emb_hi, 1)
                dve.wait_ge(s_emb_hi, g + 1)
                nc.vector.tensor_tensor(parts[:, :, 1, :], tiles, parts[:, :, 0, :], ALU.subtract).then_inc(s_emb, 1)

            def copy_embT(g):
                dve.wait_ge(s_transposed, g + 1)
                nc.vector.tensor_copy(embT[:], ps_in[:, 0:GP]).then_inc(s_embT, 1)

            def split_h2(g, j):
                dve.wait_ge(s_h2, g * J + j + 1)
                at = slice(j * P, (j + 1) * P)
                nc.vector.tensor_tensor(h2T_lo[:, at], h2T_f[:, at], h2T_hi[:, at].bitcast(F32),
                                        ALU.subtract).then_inc(s_h2_lo, 1)

            def add_rows(g, j):
                t = g * J + j
                dve.wait_ge(s_acc, t + 1)
                nc.vector.tensor_tensor(logits(t), acc[j][:, 0:N], logits(t), ALU.add).then_inc(s_acc_free, 1)

            def add_bias(t):
                nc.vector.tensor_tensor(logits(t), logits(t), bias_all[:], ALU.add).then_inc(s_biased, 1)

            def step(g, first, nth):
                split_embeddings(g + 2, first, nth)
                add_rows(g, 0)
                split_h2(g + 1, 0)
                copy_embT(g + 2)
                add_rows(g, 1)
                split_h2(g + 1, 1)

            split_embeddings(0, 0, 1)
            copy_embT(0)
            dve.wait_ge(s_bias_all, 1)
            add_bias(0)
            split_embeddings(1, J, 1)
            split_h2(0, 0)
            split_h2(0, 1)
            copy_embT(1)
            add_bias(1)
            dve.wait_ge(s_biased, 1)
            add_rows(0, 0)
            split_embeddings(2, 0, 2)
            split_h2(1, 0)
            copy_embT(2)
            dve.wait_ge(s_biased, 2)
            add_rows(0, 1)
            split_h2(1, 1)
            with dve.Fori(0, (GROUPS - 4) // 2) as i:
                step(2 * i + 1, J, i + 2)
                step(2 * i + 2, 0, i + 3)
            step(GROUPS - 3, J, TILES // IN_FLIGHT)
            add_rows(GROUPS - 2, 0)
            split_h2(GROUPS - 1, 0)
            add_bias(TILES - 1)
            add_rows(GROUPS - 2, 1)
            split_h2(GROUPS - 1, 1)
            add_rows(GROUPS - 1, 0)
            dve.wait_ge(s_biased, J + 1)
            for i, (c, n) in enumerate(chunks):
                dve.wait_ge(s_last_acc, i + 1)
                nc.vector.tensor_tensor(last_logits(c, n), acc[J - 1][:, c:c + n], last_logits(c, n),
                                        ALU.add).then_inc(s_last_sum, 1)

        @block.scalar
        def _(act):
            act.dma_start(w_hid_f[:], w_hiddenT).then_inc(s_w_hid, 16)
            act.dma_start(w1T_f[K1:2 * K1, :], w1T).then_inc(s_w1, 16)
            act.dma_start(b1_sb[:], b1.rearrange("(p a) -> p a", a=1)).then_inc(s_b1_b2, 16)
            act.dma_start(b2_sb[:], b2.rearrange("(p a) -> p a", a=1)).then_inc(s_b1_b2, 16)
            act.wait_ge(s_const, 2)
            nc.scalar.activation(warm[:], warm[:], ACT.Sigmoid)
            act.wait_ge(s_w_hid, 16)
            nc.scalar.activation(w_hid_hi[:], w_hid_f[:], ACT.Copy).then_inc(s_w_hid_hi, 1)
            act.wait_ge(s_bias_spread, 1)
            nc.scalar.activation(bias_all[:], acc[1][:, 0:N], ACT.Copy).then_inc(s_bias_all, 1)

            def relu_1(g):
                act.wait_ge(s_l1, g + 1)
                nc.scalar.activation(h1T[:], ps_in[:, 0:GP], ACT.Relu, bias=b1_sb[:]).then_inc(s_h1, 1)

            def relu_2(j):
                at = slice(j * P, (j + 1) * P)
                nc.scalar.activation(h2T_hi[:, at], ps_l2[:, at], ACT.Relu, bias=b2_sb[:])
                nc.scalar.activation(h2T_f[:, at], ps_l2[:, at], ACT.Relu, bias=b2_sb[:]).then_inc(s_h2, 1)

            def sigmoid(g, j):
                t = g * J + j
                act.wait_ge(s_acc_free, t + 1 + J)
                nc.scalar.activation(logits(t), logits(t), ACT.Sigmoid).then_inc(s_probs, 1)

            def step(g, with_l1):
                act.wait_ge(s_l2, g + 2)
                act.wait_ge(s_acc, g * J + 1)
                relu_2(0)
                sigmoid(g, 0)
                act.wait_ge(s_acc, g * J + 2)
                relu_2(1)
                if with_l1:
                    relu_1(g + 2)
                sigmoid(g, 1)

            act.wait_ge(s_b1_b2, 32)
            relu_1(0)
            act.wait_ge(s_bias_all, 1)
            act.sem_inc(s_acc_free, 1)
            act.wait_ge(s_l2, 1)
            relu_2(0)
            relu_2(1)
            relu_1(1)
            sigmoid(0, 0)
            act.wait_ge(s_l2, 2)
            act.wait_ge(s_acc, J)
            relu_2(0)
            relu_2(1)
            relu_1(2)
            sigmoid(0, 1)
            with act.Fori(1, GROUPS - 2) as g:
                step(g, True)
            step(GROUPS - 2, False)
            sigmoid(GROUPS - 1, 0)
            for i, (c, n) in enumerate(chunks):
                act.wait_ge(s_last_sum, i + 1)
                nc.scalar.activation(last_logits(c, n), last_logits(c, n), ACT.Sigmoid).then_inc(s_last_probs, 1)

        @block.tensor
        def _(pe):
            def transpose(g):
                pe.wait_ge(s_emb, g + 1)
                for j in range(J):
                    last = nc.tensor.transpose(ps_in[:, j * P:(j + 1) * P], emb[:, j * P:(j + 1) * P], ident[:])
                last.then_inc(s_transposed, 1)

            def layer_1(g):
                pe.wait_ge(s_embT, g + 1)
                nc.tensor.matmul(ps_in[:, 0:GP], w1T_hi[:], embT[:], start=True, stop=False)
                nc.tensor.matmul(ps_in[:, 0:GP], w1T_lo[:], embT[:], start=False, stop=True).then_inc(s_l1, 1)

            def layer_2(g):
                pe.wait_ge(s_h1, g + 1)
                nc.tensor.matmul(ps_l2[:, 0:GP], w2T_sb[:], h1T[:], start=True, stop=True).then_inc(s_l2, 1)

            def products(j):
                at = slice(j * P, (j + 1) * P)
                return [(h2T_hi[:, at], w_hid_hi), (h2T_hi[:, at], w_hid_lo), (h2T_lo[:, at], w_hid_hi)]

            def head(g, j, with_bias):
                t = g * J + j
                pe.wait_ge(s_acc_free, t + 1)
                pe.wait_ge(s_h2_lo, t + 1)
                terms = products(j) + ([(bias_sel[:], bias_parts)] if with_bias else [])
                for k, (h, w) in enumerate(terms):
                    for c, n in chunks:
                        last = nc.tensor.matmul(acc[j][:, c:c + n], h, w[:, c:c + n],
                                                start=(k == 0), stop=(k == len(terms) - 1))
                last.then_inc(s_acc, 1)

            def last_head():
                pe.wait_ge(s_acc_free, TILES)
                pe.wait_ge(s_h2_lo, TILES)
                terms = products(J - 1)
                for c, n in chunks:
                    for k, (h, w) in enumerate(terms):
                        last = nc.tensor.matmul(acc[J - 1][:, c:c + n], h, w[:, c:c + n],
                                                start=(k == 0), stop=(k == len(terms) - 1))
                    last.then_inc(s_last_acc, 1)

            def step(g, with_bias, with_l1):
                head(g, 0, with_bias)
                layer_2(g + 1)
                if with_l1:
                    transpose(g + 2)
                head(g, 1, with_bias)
                if with_l1:
                    layer_1(g + 2)

            pe.wait_ge(s_const, 1)
            pe.wait_ge(s_bhead, 16)
            for c, n in chunks:
                last = nc.tensor.matmul(acc[1][:, c:c + n], ones[:], bias_f[0:1, c:c + n], start=True, stop=True)
            last.then_inc(s_bias_spread, 1)
            pe.wait_ge(s_ident, 1)
            transpose(0)
            pe.wait_ge(s_w1_parts, 2)
            layer_1(0)
            pe.wait_ge(s_w2, 16)
            layer_2(0)
            transpose(1)
            pe.wait_ge(s_w_hid_lo, 1)
            pe.wait_ge(s_bias_parts, 2)
            head(0, 0, False)
            layer_1(1)
            head(0, 1, False)
            layer_2(1)
            transpose(2)
            layer_1(2)
            with pe.Fori(1, GROUPS - 2) as g:
                step(g, True, True)
            step(GROUPS - 2, True, False)
            head(GROUPS - 1, 0, True)
            last_head()


def kernel(r_interactions, L0_rec_users_emb_w, L0_rec_items_emb_w, L0_rec_w1, L0_rec_b1, L0_rec_w2, L0_rec_b2,
           L0_rec_w_head, L0_rec_b_head):
    import numpy as np
    import concourse.bacc as bacc
    from concourse.bass_utils import run_bass_kernel_spmd

    n_items = L0_rec_w_head.shape[0]
    head = np.asarray(L0_rec_w_head)
    arrays = {
        "pairs": np.asarray(r_interactions),
        "user_rows": np.asarray(L0_rec_users_emb_w),
        "item_rows": np.concatenate([np.asarray(L0_rec_items_emb_w), head[:, :n_items].T], axis=1),
        "w1T": np.asarray(L0_rec_w1).T,
        "b1": np.asarray(L0_rec_b1),
        "w2T": np.asarray(L0_rec_w2).T,
        "b2": np.asarray(L0_rec_b2),
        "w_hiddenT": head[:, n_items:].T,
        "b_head": np.asarray(L0_rec_b_head),
    }
    arrays = {name: np.ascontiguousarray(a) for name, a in arrays.items()}

    nc = bacc.Bacc("TRN2", target_bir_lowering=False, num_devices=1)
    args = [nc.dram_tensor(name, a.shape, mybir.dt.from_np(a.dtype), kind="ExternalInput").ap()
            for name, a in arrays.items()]
    args.append(nc.dram_tensor("probs", (r_interactions.shape[0], n_items), F32, kind="ExternalOutput").ap())
    rec_head_kernel(nc, *args)
    r = run_bass_kernel_spmd(nc, [arrays], core_ids=[0])
    return r.results[0]["probs"]
```
